# Optimizing a Trainium2 kernel written in Bass

```python
import numpy as np
import jax
import jax.numpy as jnp

def _softmax(x, axis=-1):
    return jax.nn.softmax(x, axis=axis)

def _gelu(x):
    return jax.nn.gelu(x, approximate=True)

def _silu(x):
    return jax.nn.silu(x)

def _sigmoid(x):
    return jax.nn.sigmoid(x)

def _layernorm(x, axis=-1, eps=1e-05):
    m = jnp.mean(x, axis=axis, keepdims=True)
    v = jnp.var(x, axis=axis, keepdims=True)
    return (x - m) / jnp.sqrt(v + eps)

def _scatter_add(tgt, idx, src, axis=0):
    return tgt.at[idx].add(src)

def _segment_sum(src, seg, n):
    return jax.ops.segment_sum(src, seg, n)
kernel_name = 'mk_pixart_seq_d2_seqx_r4_21d51e'

def setup_inputs(seed: int=0):
    np.random.seed(seed)
    _w = jnp.asarray

    def _rec_inputs():
        import jax
        import jax.numpy as jnp
        _rk = jax.random.key(seed)
        x = 7.22e-05 + 1 * jax.random.normal(jax.random.fold_in(_rk, 1), (2, 1024, 256), jnp.float32)
        _lenS = 1024 - jax.random.randint(jax.random.fold_in(_rk, 7), (2,), 0, max(1, 1024 // 4) + 1, jnp.int32)
        _lenS2 = 154 - jax.random.randint(jax.random.fold_in(_rk, 8), (2,), 0, max(1, 154 // 4) + 1, jnp.int32)
        cond_1024 = 0.000887014 + 1.03683 * jax.random.normal(jax.random.fold_in(_rk, 11), (2, 256), jnp.float32)
        _ctx_1024P = jax.random.normal(jax.random.fold_in(_rk, 12), (2, 16, 256), jnp.float32)
        _ctx_1024c = jax.random.dirichlet(jax.random.fold_in(_rk, 512), 0.3 * jnp.ones((16,), jnp.float32), (2, 154))
        _ctx_1024t = jnp.einsum('bsk,bkd->bsd', _ctx_1024c, _ctx_1024P)
        _ctx_1024t = _ctx_1024t * jax.lax.rsqrt(jnp.mean(jnp.square(_ctx_1024t)) + 1e-12) * 0.953939
        ctx_1024 = 0.00086875 + 0.999764 * (_ctx_1024t + 0.3 * jax.random.normal(jax.random.fold_in(_rk, 612), (2, 154, 256), jnp.float32))
        _validS = jnp.arange(1024)[None, :] < _lenS[:, None]
        _validS2 = jnp.arange(154)[None, :] < _lenS2[:, None]
        _causal = jnp.tril(jnp.ones((1024, 1024), dtype=bool))
        mask_BxS2_ik0 = jnp.where(jnp.broadcast_to(_validS2[:, :], (2, 154)), 0, 1).astype(jnp.int32)
        return (x, cond_1024, ctx_1024, mask_BxS2_ik0)
    x, cond_1024, ctx_1024, mask_BxS2_ik0 = _rec_inputs()

    def _L0_xcond_setup():
        import jax, jax.numpy as jnp
        import numpy as np
        C = 256
        H = 16
        D = C // H
        WIN = 128
        SHIFT = 64
        TOPK = 16
        HID = 1024
        EPS = 1e-06

        def _ln(x):
            x32 = x.astype(jnp.float32)
            m = x32.mean(-1, keepdims=True)
            v = jnp.mean((x32 - m) ** 2, axis=-1, keepdims=True)
            return ((x32 - m) * jax.lax.rsqrt(v + EPS)).astype(x.dtype)

        def _self_attn(h, w_qkv, b_qkv, w_so, b_so):
            B, L, _ = h.shape
            qkv = h @ w_qkv + b_qkv
            qkv = jnp.roll(qkv, -SHIFT, axis=1)
            nw = L // WIN
            qkv = qkv.reshape(B, nw, WIN, 3, H, D)
            q, k, v = (qkv[:, :, :, 0], qkv[:, :, :, 1], qkv[:, :, :, 2])
            scores = jnp.einsum('bnqhd,bnkhd->bnhqk', q, k) / jnp.sqrt(jnp.float32(D)).astype(h.dtype)
            attn = jax.nn.softmax(scores, axis=-1)
            o = jnp.einsum('bnhqk,bnkhd->bnqhd', attn, v).reshape(B, L, C)
            o = jnp.roll(o, SHIFT, axis=1)
            return o @ w_so + b_so

        def _topk_cross_attn(h, ctx, w_q, b_q, w_kv, b_kv, w_co, b_co):
            B, L, _ = h.shape
            Lc = ctx.shape[1]
            q = (h @ w_q + b_q).reshape(B, L, H, D)
            kv = (ctx @ w_kv + b_kv).reshape(B, Lc, 2, H, D)
            k, v = (kv[:, :, 0], kv[:, :, 1])
            scores = jnp.einsum('bqhd,bkhd->bhqk', q, k) / jnp.sqrt(jnp.float32(D)).astype(h.dtype)
            top_s, top_i = jax.lax.top_k(scores, TOPK)
            attn = jax.nn.softmax(top_s, axis=-1)
            v_bh = jnp.transpose(v, (0, 2, 1, 3))
            vg = jnp.take_along_axis(v_bh[:, :, None, :, :], top_i[..., None], axis=3)
            o = jnp.einsum('bhqk,bhqkd->bqhd', attn, vg).reshape(B, L, C)
            return o @ w_co + b_co

        def _swiglu(h, w_m1, b_m1, w_m2, b_m2):
            u = h @ w_m1 + b_m1
            a, b = (u[..., :HID], u[..., HID:])
            return jax.nn.silu(a) * b @ w_m2 + b_m2
        key = jax.random.key(seed)
        ks = jax.random.split(key, 24)
        s = 0.02
        inp = {'x': jax.random.normal(ks[0], (2, 1024, C), jnp.float32), 'mod': jax.random.normal(ks[1], (2, C), jnp.float32), 'context': jax.random.normal(ks[2], (2, 256, C), jnp.float32), 'w_ada': jax.random.normal(ks[3], (C, 9 * C), jnp.float32) * s, 'b_ada': jnp.zeros((9 * C,), jnp.float32), 'w_qkv': jax.random.normal(ks[4], (C, 3 * C), jnp.float32) * s, 'b_qkv': jnp.zeros((3 * C,), jnp.float32), 'w_so': jax.random.normal(ks[5], (C, C), jnp.float32) * s, 'b_so': jnp.zeros((C,), jnp.float32), 'w_q': jax.random.normal(ks[6], (C, C), jnp.float32) * s, 'b_q': jnp.zeros((C,), jnp.float32), 'w_kv': jax.random.normal(ks[7], (C, 2 * C), jnp.float32) * s, 'b_kv': jnp.zeros((2 * C,), jnp.float32), 'w_co': jax.random.normal(ks[8], (C, C), jnp.float32) * s, 'b_co': jnp.zeros((C,), jnp.float32), 'w_m1': jax.random.normal(ks[9], (C, 2 * HID), jnp.float32) * s, 'b_m1': jnp.zeros((2 * HID,), jnp.float32), 'w_m2': jax.random.normal(ks[10], (HID, C), jnp.float32) * s, 'b_m2': jnp.zeros((C,), jnp.float32)}
        return inp
    _L0_xcond_all = _L0_xcond_setup()
    _L0_xcond_in = {k: v for k, v in _L0_xcond_all.items() if k in ('w_ada', 'b_ada', 'w_qkv', 'b_qkv', 'w_so', 'b_so', 'w_q', 'b_q', 'w_kv', 'b_kv', 'w_co', 'b_co', 'w_m1', 'b_m1', 'w_m2', 'b_m2')}
    del _L0_xcond_all

    def _L1_xcond_setup():
        import jax, jax.numpy as jnp
        import numpy as np
        D = 256
        H = 16
        HD = D // H
        FF = 4 * D
        B, NQ, NK = (8, 256, 128)
        EPS = 1e-05

        def layernorm(x, g, b):
            m = jnp.mean(x, axis=-1, keepdims=True)
            v = jnp.mean(jnp.square(x - m), axis=-1, keepdims=True)
            return (x - m) * jax.lax.rsqrt(v + EPS) * g + b

        def mha(x, ctx, wq, bq, wk, bk, wv, bv, wo, bo, mask=None):
            Bq, Nq, _ = x.shape
            Nk = ctx.shape[1]
            q = (x @ wq + bq).reshape(Bq, Nq, H, HD)
            k = (ctx @ wk + bk).reshape(Bq, Nk, H, HD)
            v = (ctx @ wv + bv).reshape(Bq, Nk, H, HD)
            scores = jnp.einsum('bqhd,bkhd->bhqk', q, k) / np.sqrt(HD)
            if mask is not None:
                scores = jnp.where(mask[:, None, None, :].astype(bool), scores, -jnp.inf)
            attn = jax.nn.softmax(scores.astype(jnp.float32), axis=-1).astype(scores.dtype)
            out = jnp.einsum('bhqk,bkhd->bqhd', attn, v).reshape(Bq, Nq, D)
            return out @ wo + bo
        key = jax.random.key(seed)
        ks = jax.random.split(key, 40)
        rn = lambda k, shape, s=0.02: jax.random.normal(k, shape, jnp.float32) * s
        inp = {'x': jax.random.normal(ks[0], (B, NQ, D), jnp.float32), 't_emb': jax.random.normal(ks[1], (B, D), jnp.float32), 'context_emb': jax.random.normal(ks[2], (B, NK, D), jnp.float32), 'mask': jax.random.randint(ks[3], (B, NK), 0, 2, jnp.int32), 'ln1_g': jnp.ones((D,), jnp.float32), 'ln1_b': jnp.zeros((D,), jnp.float32), 'ln3_g': jnp.ones((D,), jnp.float32), 'ln3_b': jnp.zeros((D,), jnp.float32), 'ln2_g': jnp.ones((D,), jnp.float32), 'ln2_b': jnp.zeros((D,), jnp.float32), 'sa_wq': rn(ks[4], (D, D)), 'sa_bq': jnp.zeros((D,), jnp.float32), 'sa_wk': rn(ks[5], (D, D)), 'sa_bk': jnp.zeros((D,), jnp.float32), 'sa_wv': rn(ks[6], (D, D)), 'sa_bv': jnp.zeros((D,), jnp.float32), 'sa_wo': rn(ks[7], (D, D)), 'sa_bo': jnp.zeros((D,), jnp.float32), 'ca_wq': rn(ks[8], (D, D)), 'ca_bq': jnp.zeros((D,), jnp.float32), 'ca_wk': rn(ks[9], (D, D)), 'ca_bk': jnp.zeros((D,), jnp.float32), 'ca_wv': rn(ks[10], (D, D)), 'ca_bv': jnp.zeros((D,), jnp.float32), 'ca_wo': rn(ks[11], (D, D)), 'ca_bo': jnp.zeros((D,), jnp.float32), 'tp_w': rn(ks[12], (D, 3 * D)), 'tp_b': jnp.zeros((3 * D,), jnp.float32), 'w1': rn(ks[13], (D, FF)), 'b1': jnp.zeros((FF,), jnp.float32), 'w2': rn(ks[14], (FF, D)), 'b2': jnp.zeros((D,), jnp.float32)}
        return inp
    _L1_xcond_all = _L1_xcond_setup()
    _L1_xcond_in = {k: v for k, v in _L1_xcond_all.items() if k in ('ln1_g', 'ln1_b', 'ln3_g', 'ln3_b', 'ln2_g', 'ln2_b', 'sa_wq', 'sa_bq', 'sa_wk', 'sa_bk', 'sa_wv', 'sa_bv', 'sa_wo', 'sa_bo', 'ca_wq', 'ca_bq', 'ca_wk', 'ca_bk', 'ca_wv', 'ca_bv', 'ca_wo', 'ca_bo', 'tp_w', 'tp_b', 'w1', 'b1', 'w2', 'b2')}
    del _L1_xcond_all
    return {'x': x, 'cond_1024': cond_1024, 'ctx_1024': ctx_1024, 'mask_BxS2_ik0': mask_BxS2_ik0, 'L0_xcond_w_ada': _L0_xcond_in['w_ada'], 'L0_xcond_b_ada': _L0_xcond_in['b_ada'], 'L0_xcond_w_qkv': _L0_xcond_in['w_qkv'], 'L0_xcond_b_qkv': _L0_xcond_in['b_qkv'], 'L0_xcond_w_so': _L0_xcond_in['w_so'], 'L0_xcond_b_so': _L0_xcond_in['b_so'], 'L0_xcond_w_q': _L0_xcond_in['w_q'], 'L0_xcond_b_q': _L0_xcond_in['b_q'], 'L0_xcond_w_kv': _L0_xcond_in['w_kv'], 'L0_xcond_b_kv': _L0_xcond_in['b_kv'], 'L0_xcond_w_co': _L0_xcond_in['w_co'], 'L0_xcond_b_co': _L0_xcond_in['b_co'], 'L0_xcond_w_m1': _L0_xcond_in['w_m1'], 'L0_xcond_b_m1': _L0_xcond_in['b_m1'], 'L0_xcond_w_m2': _L0_xcond_in['w_m2'], 'L0_xcond_b_m2': _L0_xcond_in['b_m2'], 'L1_xcond_ln1_g': _L1_xcond_in['ln1_g'], 'L1_xcond_ln1_b': _L1_xcond_in['ln1_b'], 'L1_xcond_ln3_g': _L1_xcond_in['ln3_g'], 'L1_xcond_ln3_b': _L1_xcond_in['ln3_b'], 'L1_xcond_ln2_g': _L1_xcond_in['ln2_g'], 'L1_xcond_ln2_b': _L1_xcond_in['ln2_b'], 'L1_xcond_sa_wq': _L1_xcond_in['sa_wq'], 'L1_xcond_sa_bq': _L1_xcond_in['sa_bq'], 'L1_xcond_sa_wk': _L1_xcond_in['sa_wk'], 'L1_xcond_sa_bk': _L1_xcond_in['sa_bk'], 'L1_xcond_sa_wv': _L1_xcond_in['sa_wv'], 'L1_xcond_sa_bv': _L1_xcond_in['sa_bv'], 'L1_xcond_sa_wo': _L1_xcond_in['sa_wo'], 'L1_xcond_sa_bo': _L1_xcond_in['sa_bo'], 'L1_xcond_ca_wq': _L1_xcond_in['ca_wq'], 'L1_xcond_ca_bq': _L1_xcond_in['ca_bq'], 'L1_xcond_ca_wk': _L1_xcond_in['ca_wk'], 'L1_xcond_ca_bk': _L1_xcond_in['ca_bk'], 'L1_xcond_ca_wv': _L1_xcond_in['ca_wv'], 'L1_xcond_ca_bv': _L1_xcond_in['ca_bv'], 'L1_xcond_ca_wo': _L1_xcond_in['ca_wo'], 'L1_xcond_ca_bo': _L1_xcond_in['ca_bo'], 'L1_xcond_tp_w': _L1_xcond_in['tp_w'], 'L1_xcond_tp_b': _L1_xcond_in['tp_b'], 'L1_xcond_w1': _L1_xcond_in['w1'], 'L1_xcond_b1': _L1_xcond_in['b1'], 'L1_xcond_w2': _L1_xcond_in['w2'], 'L1_xcond_b2': _L1_xcond_in['b2']}

def reference(x, cond_1024, ctx_1024, mask_BxS2_ik0, L0_xcond_w_ada, L0_xcond_b_ada, L0_xcond_w_qkv, L0_xcond_b_qkv, L0_xcond_w_so, L0_xcond_b_so, L0_xcond_w_q, L0_xcond_b_q, L0_xcond_w_kv, L0_xcond_b_kv, L0_xcond_w_co, L0_xcond_b_co, L0_xcond_w_m1, L0_xcond_b_m1, L0_xcond_w_m2, L0_xcond_b_m2, L1_xcond_ln1_g, L1_xcond_ln1_b, L1_xcond_ln3_g, L1_xcond_ln3_b, L1_xcond_ln2_g, L1_xcond_ln2_b, L1_xcond_sa_wq, L1_xcond_sa_bq, L1_xcond_sa_wk, L1_xcond_sa_bk, L1_xcond_sa_wv, L1_xcond_sa_bv, L1_xcond_sa_wo, L1_xcond_sa_bo, L1_xcond_ca_wq, L1_xcond_ca_bq, L1_xcond_ca_wk, L1_xcond_ca_bk, L1_xcond_ca_wv, L1_xcond_ca_bv, L1_xcond_ca_wo, L1_xcond_ca_bo, L1_xcond_tp_w, L1_xcond_tp_b, L1_xcond_w1, L1_xcond_b1, L1_xcond_w2, L1_xcond_b2):
    import jax
    import jax.numpy as jnp

    def _L0_xcond_ref(x, mod, context, w_ada, b_ada, w_qkv, b_qkv, w_so, b_so, w_q, b_q, w_kv, b_kv, w_co, b_co, w_m1, b_m1, w_m2, b_m2):
        import jax, jax.numpy as jnp
        import numpy as np
        C = 256
        H = 16
        D = C // H
        WIN = 128
        SHIFT = 64
        TOPK = 16
        HID = 1024
        EPS = 1e-06

        def _ln(x):
            x32 = x.astype(jnp.float32)
            m = x32.mean(-1, keepdims=True)
            v = jnp.mean((x32 - m) ** 2, axis=-1, keepdims=True)
            return ((x32 - m) * jax.lax.rsqrt(v + EPS)).astype(x.dtype)

        def _self_attn(h, w_qkv, b_qkv, w_so, b_so):
            B, L, _ = h.shape
            qkv = h @ w_qkv + b_qkv
            qkv = jnp.roll(qkv, -SHIFT, axis=1)
            nw = L // WIN
            qkv = qkv.reshape(B, nw, WIN, 3, H, D)
            q, k, v = (qkv[:, :, :, 0], qkv[:, :, :, 1], qkv[:, :, :, 2])
            scores = jnp.einsum('bnqhd,bnkhd->bnhqk', q, k) / jnp.sqrt(jnp.float32(D)).astype(h.dtype)
            attn = jax.nn.softmax(scores, axis=-1)
            o = jnp.einsum('bnhqk,bnkhd->bnqhd', attn, v).reshape(B, L, C)
            o = jnp.roll(o, SHIFT, axis=1)
            return o @ w_so + b_so

        def _topk_cross_attn(h, ctx, w_q, b_q, w_kv, b_kv, w_co, b_co):
            B, L, _ = h.shape
            Lc = ctx.shape[1]
            q = (h @ w_q + b_q).reshape(B, L, H, D)
            kv = (ctx @ w_kv + b_kv).reshape(B, Lc, 2, H, D)
            k, v = (kv[:, :, 0], kv[:, :, 1])
            scores = jnp.einsum('bqhd,bkhd->bhqk', q, k) / jnp.sqrt(jnp.float32(D)).astype(h.dtype)
            top_s, top_i = jax.lax.top_k(scores, TOPK)
            attn = jax.nn.softmax(top_s, axis=-1)
            v_bh = jnp.transpose(v, (0, 2, 1, 3))
            vg = jnp.take_along_axis(v_bh[:, :, None, :, :], top_i[..., None], axis=3)
            o = jnp.einsum('bhqk,bhqkd->bqhd', attn, vg).reshape(B, L, C)
            return o @ w_co + b_co

        def _swiglu(h, w_m1, b_m1, w_m2, b_m2):
            u = h @ w_m1 + b_m1
            a, b = (u[..., :HID], u[..., HID:])
            return jax.nn.silu(a) * b @ w_m2 + b_m2
        m = jax.nn.silu(mod) @ w_ada + b_ada
        sh_msa, sc_msa, g_msa, sh_mca, sc_mca, g_mca, sh_mlp, sc_mlp, g_mlp = [m[:, i * C:(i + 1) * C][:, None, :] for i in range(9)]
        h = _ln(x) * (1 + sc_msa) + sh_msa
        h = _self_attn(h, w_qkv, b_qkv, w_so, b_so)
        x = x + h * g_msa
        h = _ln(x) * (1 + sc_mca) + sh_mca
        h = _topk_cross_attn(h, context, w_q, b_q, w_kv, b_kv, w_co, b_co)
        x = x + h * g_mca
        h = _ln(x) * (1 + sc_mlp) + sh_mlp
        h = _swiglu(h, w_m1, b_m1, w_m2, b_m2)
        x = x + h * g_mlp
        return x

    def _L1_xcond_ref(x, t_emb, context_emb, mask, ln1_g, ln1_b, ln3_g, ln3_b, ln2_g, ln2_b, sa_wq, sa_bq, sa_wk, sa_bk, sa_wv, sa_bv, sa_wo, sa_bo, ca_wq, ca_bq, ca_wk, ca_bk, ca_wv, ca_bv, ca_wo, ca_bo, tp_w, tp_b, w1, b1, w2, b2):
        import jax, jax.numpy as jnp
        import numpy as np
        D = 256
        H = 16
        HD = D // H
        FF = 4 * D
        B, NQ, NK = (8, 256, 128)
        EPS = 1e-05

        def layernorm(x, g, b):
            m = jnp.mean(x, axis=-1, keepdims=True)
            v = jnp.mean(jnp.square(x - m), axis=-1, keepdims=True)
            return (x - m) * jax.lax.rsqrt(v + EPS) * g + b

        def mha(x, ctx, wq, bq, wk, bk, wv, bv, wo, bo, mask=None):
            Bq, Nq, _ = x.shape
            Nk = ctx.shape[1]
            q = (x @ wq + bq).reshape(Bq, Nq, H, HD)
            k = (ctx @ wk + bk).reshape(Bq, Nk, H, HD)
            v = (ctx @ wv + bv).reshape(Bq, Nk, H, HD)
            scores = jnp.einsum('bqhd,bkhd->bhqk', q, k) / np.sqrt(HD)
            if mask is not None:
                scores = jnp.where(mask[:, None, None, :].astype(bool), scores, -jnp.inf)
            attn = jax.nn.softmax(scores.astype(jnp.float32), axis=-1).astype(scores.dtype)
            out = jnp.einsum('bhqk,bkhd->bqhd', attn, v).reshape(Bq, Nq, D)
            return out @ wo + bo
        t_biases = jax.nn.silu(t_emb) @ tp_w + tp_b
        t_sa, t_ca, t_mlp = jnp.split(t_biases, 3, axis=-1)
        h = layernorm(x, ln1_g, ln1_b)
        h = mha(h, h, sa_wq, sa_bq, sa_wk, sa_bk, sa_wv, sa_bv, sa_wo, sa_bo)
        x = x + h + t_sa[:, None, :]
        h = layernorm(x, ln3_g, ln3_b)
        h = mha(h, context_emb, ca_wq, ca_bq, ca_wk, ca_bk, ca_wv, ca_bv, ca_wo, ca_bo, mask=mask)
        x = x + h + t_ca[:, None, :]
        h = layernorm(x, ln2_g, ln2_b)
        h = jax.nn.gelu(h @ w1 + b1, approximate=False) @ w2 + b2
        x = x + h + t_mlp[:, None, :]
        return x
    x = _L0_xcond_ref(x, cond_1024, ctx_1024, L0_xcond_w_ada, L0_xcond_b_ada, L0_xcond_w_qkv, L0_xcond_b_qkv, L0_xcond_w_so, L0_xcond_b_so, L0_xcond_w_q, L0_xcond_b_q, L0_xcond_w_kv, L0_xcond_b_kv, L0_xcond_w_co, L0_xcond_b_co, L0_xcond_w_m1, L0_xcond_b_m1, L0_xcond_w_m2, L0_xcond_b_m2)
    x = _L1_xcond_ref(x, cond_1024, ctx_1024, mask_BxS2_ik0, L1_xcond_ln1_g, L1_xcond_ln1_b, L1_xcond_ln3_g, L1_xcond_ln3_b, L1_xcond_ln2_g, L1_xcond_ln2_b, L1_xcond_sa_wq, L1_xcond_sa_bq, L1_xcond_sa_wk, L1_xcond_sa_bk, L1_xcond_sa_wv, L1_xcond_sa_bv, L1_xcond_sa_wo, L1_xcond_sa_bo, L1_xcond_ca_wq, L1_xcond_ca_bq, L1_xcond_ca_wk, L1_xcond_ca_bk, L1_xcond_ca_wv, L1_xcond_ca_bv, L1_xcond_ca_wo, L1_xcond_ca_bo, L1_xcond_tp_w, L1_xcond_tp_b, L1_xcond_w1, L1_xcond_b1, L1_xcond_w2, L1_xcond_b2)
    return x

_drawn_inputs = setup_inputs


def setup_inputs(seed=0):
    import zlib

    import numpy as np

    out = dict(_drawn_inputs(seed))
    spreads = {'L0_xcond_b_ada': (0.0, 0.417),
     'L0_xcond_b_qkv': (0.0, 0.8),
     'L0_xcond_b_so': (0.0, 0.393),
     'L0_xcond_b_q': (0.0, 0.8),
     'L0_xcond_b_kv': (0.0, 0.8),
     'L0_xcond_b_co': (0.0, 0.394),
     'L0_xcond_b_m1': (0.0, 0.8),
     'L0_xcond_b_m2': (0.0, 1.609),
     'L1_xcond_ln1_g': (1.0, 0.6),
     'L1_xcond_ln1_b': (0.0, 0.708),
     'L1_xcond_ln3_g': (1.0, 0.6),
     'L1_xcond_ln3_b': (0.0, 2.0),
     'L1_xcond_ln2_g': (1.0, 0.6),
     'L1_xcond_ln2_b': (0.0, 2.0),
     'L1_xcond_sa_bq': (0.0, 0.8),
     'L1_xcond_sa_bk': (0.0, 2.0),
     'L1_xcond_sa_bv': (0.0, 0.8),
     'L1_xcond_sa_bo': (0.0, 0.8),
     'L1_xcond_ca_bq': (0.0, 2.0),
     'L1_xcond_ca_bk': (0.0, 2.0),
     'L1_xcond_ca_bv': (0.0, 2.0),
     'L1_xcond_ca_bo': (0.0, 0.778),
     'L1_xcond_tp_b': (0.0, 0.464),
     'L1_xcond_b1': (0.0, 0.8),
     'L1_xcond_b2': (0.0, 0.783)}
    factors = {'L0_xcond_w_qkv': 8.0,
     'L0_xcond_w_so': 6.215,
     'L0_xcond_w_q': 5.785,
     'L0_xcond_w_kv': 3.675,
     'L0_xcond_w_co': 3.227,
     'L0_xcond_w_m1': 6.382,
     'L0_xcond_w_m2': 6.352,
     'L1_xcond_sa_wq': 8.0,
     'L1_xcond_sa_wk': 8.0,
     'L1_xcond_sa_wv': 4.704,
     'L1_xcond_ca_wq': 51.084,
     'L1_xcond_ca_wk': 50.642,
     'L1_xcond_ca_wv': 5.33,
     'L1_xcond_ca_wo': 4.157,
     'L1_xcond_w1': 3.225,
     'L1_xcond_w2': 2.915}
    for name, (base, spread) in spreads.items():
        noise = np.random.default_rng([zlib.crc32(name.encode()), seed]).standard_normal(out[name].shape)
        drawn = base * np.exp(spread * noise) if base else spread * noise
        out[name] = jnp.asarray(drawn.astype(out[name].dtype))
    for name, factor in factors.items():
        out[name] = (out[name] * factor).astype(out[name].dtype)
    return out
```

```python
from contextlib import ExitStack

import concourse.bass as bass
from concourse import mybir

F32 = mybir.dt.float32
BF16 = mybir.dt.bfloat16
I32 = mybir.dt.int32
ALU = mybir.AluOpType
ACT = mybir.ActivationFunctionType
AX = mybir.AxisListType
ds = bass.ds

B, L, C, H, D = 2, 1024, 256, 16, 16
P = 128
TB = L // P
TILES = B * TB
CK = C // P
BLK = 4
BT = BLK * P
NB = TILES // BLK
HG = 4
HW = 32
G = B * H // HG
SHIFT = 64
HID = 1024
S2 = 154
TAIL = S2 - P
TOPK = 16
SCALE = 0.25
Q_PART = (0, 1, 0, 2, 1, 0)
K_PART = (0, 0, 1, 0, 1, 2)
PACK = 16 * len(Q_PART)
FAR = 1e30


def wait(eng, sem, value):
    if not (isinstance(value, int) and value <= 0):
        eng.wait_ge(sem, value)


def stage_semaphores(nc, ctx, prefix=""):
    taken = []

    def new(name):
        taken.append(nc.alloc_semaphore(prefix + name))
        return taken[-1]

    def clear():
        nc.clear_and_free_semaphores(taken)
        nc.all_engine_barrier(sem_only=True)

    ctx.callback(clear)
    return new


def wait_apart(eng, sem, value, passed):
    eng.wait_ge(sem, value)
    eng.sem_inc(passed, 1)


class Chain:

    def __init__(self, eng, sem, start=0):
        self.eng, self.sem, self.n = eng, sem, start

    def link(self, instruction):
        instruction.then_inc(self.sem, 1)
        self.n = self.n + 1
        self.eng.wait_ge(self.sem, self.n)


def each_group(eng, turns, body):
    body(0, 0, True, False)
    with eng.Fori(0, (G - 2) // turns, 1) as i:
        for j in range(turns):
            body(i * turns + (j + 1), (j + 1) % turns, False, False)
    body(G - 1, (G - 1) % turns, False, True)


COLUMNS = [("L0_xcond_" + name, n) for name, n in (("b_ada", 18), ("b_qkv", 6), ("b_q", 2), ("b_kv", 4), ("b_m1", 16))] + \
    [("L1_xcond_" + name, n) for name, n in (("sa_bq", 2), ("sa_bk", 2), ("ca_bq", 2), ("ca_bk", 2), ("b1", 8), ("ln1_g", 2),
                                             ("ln1_b", 2), ("ln3_g", 2), ("ln3_b", 2), ("ln2_g", 2), ("ln2_b", 2))]


class Memory:
    pass


def interleave(main, side):
    out, done = [], 0
    for i, step in enumerate(main):
        upto = (i * len(side)) // max(len(main), 1)
        out += side[done:upto]
        done = max(done, upto)
        out.append(step)
    return out + side[done:]



def modulation_stage(nc, m, a):
    L0, L1 = "L0_xcond_", "L1_xcond_"
    with ExitStack() as ctx:
        sb = lambda name, shape, dt=F32: ctx.enter_context(nc.sbuf_tensor(name, shape, dt))
        sem = stage_semaphores(nc, ctx)
        w_ada = sb("w_ada", [P, CK, 9 * C])
        w_tp = sb("w_tp", [P, CK, 3 * C])
        cond = sb("cond", [P, CK, B])
        silu_c = sb("silu_c", [P, CK, B])
        silu_wide = sb("silu_wide", [P, CK, B, P])
        ada_row = sb("ada_row", [P, 3, C])
        tp_row = sb("tp_row", [P, 3, C])
        gate = sb("gate", [P, 3, B, C])
        out_row = sb("out_row", [P, 6, C])
        ps = [ctx.enter_context(nc.psum_tensor(f"mod_ps{i}", [P, 512], F32)) for i in range(3)]
        cond_in, small_in, ada_in, rows_in = sem("cond_in"), sem("small_in"), sem("ada_in"), sem("rows_in")
        silu_done, wide_done = sem("silu_done"), sem("wide_done")
        col_mm, row_mm, row_read, mod_chain, ident_0 = sem("col_mm"), sem("row_mm"), sem("row_read"), sem("mod_chain"), sem("ident_0")
        plain_row = (L0 + "b_so", L0 + "b_co", L0 + "b_m2", L1 + "sa_bo", L1 + "ca_bo", L1 + "b2")
        with nc.Block() as block:

            @block.sync
            def _(sp):
                sp.dma_start(cond[:, :, :], a["cond_columns"]).then_inc(cond_in, 16)
                for k in range(CK):
                    sp.dma_start(w_ada[:, k, :], a[L0 + "w_ada"][k * P:(k + 1) * P, :]).then_inc(ada_in, 16)
                sp.dma_start(w_tp[:, :, :], a[L1 + "tp_w"].rearrange("(k p) n -> p k n", p=P)).then_inc(ada_in, 16)
                for b in range(B):
                    sp.dma_start(m.x[:, b * TB:(b + 1) * TB - 1, :],
                                 a["x"][b, SHIFT:L - SHIFT, :].rearrange("(t p) c -> p t c", p=P)).then_inc(m.x_in, 16)
                    sp.dma_start(m.x[0:P - SHIFT, (b + 1) * TB - 1, :], a["x"][b, L - SHIFT:L, :]).then_inc(m.x_in, 16)
                    sp.dma_start(m.x[P - SHIFT:P, (b + 1) * TB - 1, :], a["x"][b, 0:SHIFT, :]).then_inc(m.x_in, 16)
                for name, tile in m.weights:
                    sp.dma_start(tile, a[name].rearrange("(k p) n -> p k n", p=P)).then_inc(m.w_in[name], 16)

            @block.gpsimd
            def _(pool):
                nc.gpsimd.memset(m.ident[:, :], 0.0).then_inc(ident_0, 1)
                pool.wait_ge(ident_0, 1)
                nc.gpsimd.affine_select(out=m.ident[:, :], in_=m.ident[:, :], compare_op=ALU.not_equal, fill=1.0,
                                        base=0, pattern=[[-1, P]], channel_multiplier=1).then_inc(m.ident_in, 1)

            @block.scalar
            def _(act):
                act.dma_start(m.columns[:, :], a["columns"]).then_inc(small_in, 16)
                for i in range(3):
                    act.dma_start(ada_row[:, i, :], a[L0 + "b_ada"][(3 * i + 2) * C:(3 * i + 3) * C].partition_broadcast(P)).then_inc(rows_in, 16)
                    act.dma_start(tp_row[:, i, :], a[L1 + "tp_b"][i * C:(i + 1) * C].partition_broadcast(P)).then_inc(rows_in, 16)
                for i, name in enumerate(plain_row):
                    act.dma_start(out_row[:, i, :], a[name].partition_broadcast(P)).then_inc(rows_in, 16)
                for tile, source in m.value_rows:
                    act.dma_start(tile, source.partition_broadcast(P)).then_inc(rows_in, 16)
                act.wait_ge(cond_in, 16)
                nc.scalar.activation(silu_c[:, :, :], cond[:, :, :], ACT.Silu).then_inc(silu_done, 1)

            @block.tensor
            def _(pe):
                pe.wait_ge(silu_done, 1)
                pe.wait_ge(ada_in, 16 * (CK + 1))
                last = None
                for c in range(18):
                    for k in range(CK):
                        last = nc.tensor.matmul(ps[0][:, B * c:B * c + B], w_ada[:, k, c * P:(c + 1) * P], silu_c[:, k, :],
                                                start=(k == 0), stop=(k == CK - 1))
                last.then_inc(col_mm, 1)
                pe.wait_ge(wide_done, 1)
                n = 0
                for w, chunk in ((w_ada, lambda i: 3 * i + 2), (w_tp, lambda i: i)):
                    for i in range(3):
                        for b in range(B):
                            wait(pe, row_read, n - 1)
                            for k in range(CK):
                                last = nc.tensor.matmul(ps[1 + n % 2][:, 0:C], silu_wide[:, k, b, :],
                                                        w[:, k, chunk(i) * C:(chunk(i) + 1) * C], start=(k == 0), stop=(k == CK - 1))
                            last.then_inc(row_mm, 1)
                            n += 1

            @block.vector
            def _(dve):
                chain = Chain(dve, mod_chain)
                dve.wait_ge(silu_done, 1)
                nc.vector.tensor_copy(silu_wide[:, :, :, :].rearrange("p k b n -> p (k b) n"),
                                      silu_c[:, :, :].rearrange("p k b -> p (k b)").unsqueeze(2).to_broadcast([P, CK * B, P])).then_inc(wide_done, 1)
                dve.wait_ge(small_in, 16)
                for tile in m.query_columns:
                    chain.link(nc.vector.tensor_scalar(tile, tile, SCALE, None, ALU.mult))
                dve.wait_ge(col_mm, 1)
                for b in range(B):
                    chain.link(nc.vector.tensor_tensor(m.mod[:, :, b], ps[0][:, 0:18 * B].rearrange("p (c b) -> p c b", b=B)[:, :, b],
                                                       m.ada_col, ALU.add))
                for i in range(3):
                    c = (3 * i + 1) * CK
                    chain.link(nc.vector.tensor_scalar(m.mod[:, c:c + CK, :], m.mod[:, c:c + CK, :], 1.0, None, ALU.add))
                dve.wait_ge(rows_in, 16 * (12 + len(m.value_rows)))
                n = 0
                for i in range(3):
                    for b in range(B):
                        dve.wait_ge(row_mm, n + 1)
                        nc.vector.tensor_tensor(gate[:, i, b, :], ps[1 + n % 2][:, 0:C], ada_row[:, i, :], ALU.add).then_inc(row_read, 1)
                        n += 1
                        dve.wait_ge(row_read, n)
                        nc.vector.tensor_tensor(m.res_row[:, i, b, :], gate[:, i, b, :], out_row[:, i, :], ALU.mult)
                for i in range(3):
                    dve.wait_ge(m.w_in[m.gated[i][0]], 16)
                    for b in range(B):
                        raw, folded = m.gated[i][1], m.gated[i][2][b]
                        for k in range(raw.shape[1]):
                            nc.vector.tensor_tensor(folded[:, k, :], raw[:, k, :], gate[:, i, b, :], ALU.mult)
                for i in range(3):
                    for b in range(B):
                        dve.wait_ge(row_mm, n + 1)
                        nc.vector.tensor_tensor(m.res_row[:, 3 + i, b, :], ps[1 + n % 2][:, 0:C], tp_row[:, i, :], ALU.add).then_inc(row_read, 1)
                        n += 1
                        dve.wait_ge(row_read, n)
                        chain.link(nc.vector.tensor_tensor(m.res_row[:, 3 + i, b, :], m.res_row[:, 3 + i, b, :], out_row[:, 3 + i, :], ALU.add))



def context_stage(nc, m, a):
    with ExitStack() as ctx:
        sb = lambda name, shape, dt=F32: ctx.enter_context(nc.sbuf_tensor(name, shape, dt))
        sem = stage_semaphores(nc, ctx)
        psum = lambda name: ctx.enter_context(nc.psum_tensor(name, [P, 512], F32))
        rows = sb("ctx_rows", [P, 2, B, C])
        ctx_t = sb("ctx_t", [P, CK, B * S2])
        full = sb("ctx_k_full", [P, B * S2])
        rest = sb("ctx_k_rest", [P, B * S2])
        parts = sb("ctx_k_parts", [P, 2, 3, B * S2], BF16)
        v_out = sb("ctx_v_out", [P, 2, H, HW])
        v_masked = sb("ctx_v_masked", [P, 2, H, HW])
        mask_i = sb("mask_i", [P, 2, B], I32)
        mask_c = sb("mask_c", [P, 2, B])
        mrow_i = sb("mrow_i", [1, B * S2], I32)
        mrow = sb("mrow", [1, B * S2])
        mrow_b = sb("mrow_b", [1, HG, B * S2], BF16)
        t_ps = [psum(f"ctx_t_ps{k}") for k in range(CK)]
        k_ps = [psum(f"ctx_k_ps{i}") for i in range(2)]
        v_ps = [psum(f"ctx_v_ps{i}") for i in range(2)]
        ctx_in, mask_in = sem("ctx_in"), sem("mask_in")
        t_mm, t_done, k_mm, k_full, k_hi, k_rest, k_parts = (sem("ctx_" + s) for s in ("t_mm", "t_done", "k_mm", "k_full", "k_hi", "k_rest", "k_parts"))
        v_mm, v_done, chain_sem, ones_done, mask_done = (sem("ctx_" + s) for s in ("v_mm", "v_done", "chain", "ones", "mask"))
        k_stored = [sem(f"ctx_k_stored{i}") for i in range(2)]
        v_stored = [sem(f"ctx_v_stored{i}") for i in range(2)]
        mask_stored = sem("mask_stored")
        K_UNITS = [(x, mt) for x in range(2) for mt in range(CK)]
        V_UNITS = [(x, b, tail) for x in range(2) for b in range(B) for tail in range(2)]
        with nc.Block() as block:

            @block.sync
            def _(sp):
                for b in range(B):
                    sp.dma_start(rows[:, 0, b, :], a["ctx_1024"][b, 0:P, :]).then_inc(ctx_in, 16)
                    sp.dma_start(rows[0:TAIL, 1, b, :], a["ctx_1024"][b, P:S2, :]).then_inc(ctx_in, 16)
                mk = a["mask_BxS2_ik0"]
                sp.dma_start(mask_i[:, 0, :], a["mask_columns"][0:P, :]).then_inc(mask_in, 16)
                sp.dma_start(mask_i[0:TAIL, 1, :], a["mask_columns"][P:S2, :]).then_inc(mask_in, 16)
                sp.dma_start(mrow_i[:, :], mk.rearrange("b s -> (b s)").unsqueeze(0)).then_inc(mask_in, 16)
                for u, (x, mt) in enumerate(K_UNITS):
                    sp.wait_ge(k_parts, u + 1)
                    for b in range(B):
                        sp.dma_start(m.ctx_k[x][:, b * C + mt * P:b * C + (mt + 1) * P, :].rearrange("s r t -> r s t"),
                                     parts[:, u % 2, :, b * S2:(b + 1) * S2]).then_inc(k_stored[u % 2], 16)
                for u, (x, b, tail) in enumerate(V_UNITS):
                    sp.wait_ge(v_done, u + 1)
                    n = TAIL if tail else P
                    sp.dma_start(m.ctx_v[x][b * HG:(b + 1) * HG, tail * P:tail * P + n, :].rearrange("g p e -> p g e"),
                                 (v_masked if x else v_out)[0:n, u % 2, :, :].rearrange("p (g h) e -> p g (h e)", g=HG)).then_inc(v_stored[u % 2], 16)
                sp.wait_ge(mask_done, 1)
                for n in range(G):
                    b = n // HG
                    sp.dma_start(m.ctx_mask[n:n + 1, :, :], mrow_b[0:1, :, b * S2:(b + 1) * S2]).then_inc(mask_stored, 16)
                for i in range(2):
                    sp.wait_ge(k_stored[i], 16 * B * len(K_UNITS) // 2)
                    sp.wait_ge(v_stored[i], 16 * len(V_UNITS) // 2)
                sp.wait_ge(mask_stored, 16 * G)

            @block.gpsimd
            def _(pool):
                nc.gpsimd.memset(v_out[:, :, :, D:HW], 1.0).then_inc(ones_done, 1)

            @block.tensor
            def _(pe):
                pe.wait_ge(ctx_in, 16 * 2 * B)
                pe.wait_ge(m.ident_in, 1)
                for k in range(CK):
                    for b in range(B):
                        nc.tensor.transpose(t_ps[k][:, b * S2:b * S2 + P], rows[:, 0, b, k * P:(k + 1) * P], m.ident[:, :])
                        last = nc.tensor.transpose(t_ps[k][:, b * S2 + P:(b + 1) * S2], rows[0:TAIL, 1, b, k * P:(k + 1) * P],
                                                   m.ident[0:TAIL, 0:TAIL])
                    last.then_inc(t_mm, 1)
                pe.wait_ge(t_done, CK)
                for u, (x, mt) in enumerate(K_UNITS):
                    w, name = m.ctx_wk[x]
                    pe.wait_ge(m.w_in[name], 16)
                    wait(pe, k_hi, u - 1)
                    for k in range(CK):
                        last = nc.tensor.matmul(k_ps[u % 2][:, 0:B * S2], w[:, k, mt * P:(mt + 1) * P], ctx_t[:, k, :],
                                                start=(k == 0), stop=(k == CK - 1))
                    last.then_inc(k_mm, 1)
                for u, (x, b, tail) in enumerate(V_UNITS):
                    w, name = m.ctx_wv[x]
                    pe.wait_ge(m.w_in[name], 16)
                    wait(pe, v_done, u - 1)
                    n, t0 = (TAIL if tail else P), b * S2 + tail * P
                    for k in range(CK):
                        last = nc.tensor.matmul(v_ps[u % 2][0:n, 0:C], ctx_t[:, k, t0:t0 + n], w[:, k, :],
                                                start=(k == 0), stop=(k == CK - 1))
                    last.then_inc(v_mm, 1)

            @block.scalar
            def _(act):
                for k in range(CK):
                    act.wait_ge(t_mm, k + 1)
                    nc.scalar.activation(ctx_t[:, k, :], t_ps[k][:, 0:B * S2], ACT.Copy).then_inc(t_done, 1)
                for u, (x, mt) in enumerate(K_UNITS):
                    act.wait_ge(k_mm, u + 1)
                    wait(act, k_parts, u)
                    wait(act, k_stored[u % 2], 16 * B * (u // 2))
                    bias = m.ctx_k_bias[x][:, mt:mt + 1]
                    nc.scalar.activation(full[:, :], k_ps[u % 2][:, 0:B * S2], ACT.Identity, bias=bias).then_inc(k_full, 1)
                    nc.scalar.activation(parts[:, u % 2, 0, :], k_ps[u % 2][:, 0:B * S2], ACT.Identity, bias=bias).then_inc(k_hi, 1)

            @block.vector
            def _(dve):
                chain = Chain(dve, chain_sem)
                dve.wait_ge(mask_in, 48)
                nc.vector.tensor_scalar(mask_c[:, 0, :], mask_i[:, 0, :], 0, None, ALU.not_equal)
                chain.link(nc.vector.tensor_scalar(mask_c[0:TAIL, 1, :], mask_i[0:TAIL, 1, :], 0, None, ALU.not_equal))
                chain.link(nc.vector.tensor_scalar(mrow[:, :], mrow_i[:, :], 0, -FAR, ALU.is_equal, ALU.mult))
                for h in range(HG):
                    last = nc.vector.tensor_copy(mrow_b[:, h, :], mrow[:, :])
                last.then_inc(mask_done, 1)
                for u, (x, mt) in enumerate(K_UNITS):
                    dve.wait_ge(k_full, u + 1)
                    dve.wait_ge(k_hi, u + 1)
                    chain.link(nc.vector.tensor_tensor(rest[:, :], full[:, :], parts[:, u % 2, 0, :], ALU.subtract))
                    chain.link(nc.vector.tensor_copy(parts[:, u % 2, 1, :], rest[:, :]))
                    nc.vector.tensor_tensor(parts[:, u % 2, 2, :], rest[:, :], parts[:, u % 2, 1, :], ALU.subtract).then_inc(k_parts, 1)
                dve.wait_ge(ones_done, 1)
                for u, (x, b, tail) in enumerate(V_UNITS):
                    n = TAIL if tail else P
                    dve.wait_ge(v_mm, u + 1)
                    wait(dve, v_stored[u % 2], 16 * (u // 2))
                    sum_ = nc.vector.tensor_tensor(v_out[0:n, u % 2, :, 0:D], v_ps[u % 2][0:n, 0:C].rearrange("p (h d) -> p h d", d=D),
                                                   m.ctx_v_row[x][0:n, :].rearrange("p (h d) -> p h d", d=D), ALU.add)
                    if x == 0:
                        sum_.then_inc(v_done, 1)
                    else:
                        chain.link(sum_)
                        nc.vector.tensor_scalar(v_masked[0:n, u % 2, :, :].rearrange("p h e -> p (h e)"),
                                                v_out[0:n, u % 2, :, :].rearrange("p h e -> p (h e)"),
                                                mask_c[0:n, tail, b:b + 1], None, ALU.mult).then_inc(v_done, 1)



class TokenStage:

    def __init__(self, nc, m, ctx, name, spec):
        self.nc, self.m, self.s = nc, m, spec
        self.sb = lambda n, shape, dt=F32: ctx.enter_context(nc.sbuf_tensor(name + n, shape, dt))
        self.sem = stage_semaphores(nc, ctx, name)
        psum = lambda n: ctx.enter_context(nc.psum_tensor(name + n, [P, 512], F32))
        self.o_bank, self.n_bank, self.y_bank = psum("o_bank"), psum("n_bank"), psum("y_bank")
        self.h_bank = [psum(f"h_bank{k}") for k in range(CK)]
        self.p_bank = [psum(f"p_bank{k}") for k in range(3)]
        self.recip = self.sb("recip", [P, 2, H])
        self.o_norm = self.sb("o_norm", [P, 2, C])
        self.o_norm_t = self.sb("o_norm_t", [P, 2, CK, P])
        self.stats = self.sb("stats", [P, 6])
        self.mean_var = self.sb("mean_var", [P, TILES, 2])
        self.rstd = self.sb("rstd", [P, TILES])
        self.var_eps = self.sb("var_eps", [P, TILES])
        self.power = self.sb("power", [P, 1])
        self.x_hat = self.sb("x_hat", [P, 2, C])
        self.h_t = self.sb("h_t", [P, 2, CK, BT])
        self.o_turned, self.o_normed = self.sem("o_turned"), self.sem("o_normed")
        self.on_turned, self.on_copied = self.sem("on_turned"), self.sem("on_copied")
        self.y_mm, self.row_added, self.x_summed = self.sem("y_mm"), self.sem("row_added"), self.sem("x_summed")
        self.x_stats, self.rstd_done, self.hat_done = self.sem("x_stats"), self.sem("rstd_done"), self.sem("hat_done")
        self.hat_turned, self.h_done = self.sem("hat_turned"), self.sem("h_done")
        self.dve_chain, self.pool_chain = self.sem("dve_chain"), self.sem("pool_chain")

    def attention_steps(self, block):
        tiles = range(block * BLK, (block + 1) * BLK)
        if not self.s["attended"]:
            return [step for t in tiles for step in (("stats", t), ("hat_turn", t))] + [("modulate", block)]
        out = []
        for s in range(BLK + 3):
            for lag, names in ((0, ("o_turn", "o_norm")), (1, ("on_turn", "on_copy")), (2, ("y_mm", "x_sum", "stats")), (3, ("hat_turn",))):
                t = s - lag
                if 0 <= t < BLK:
                    out += [(n, block * BLK + t) for n in names]
        return out + [("modulate", block)]

    def tensor_step(self, pe, kind, t):
        nc, m, s = self.nc, self.m, self.s
        b, tb = t // TB, t % TB
        if kind == "o_turn":
            wait(pe, self.o_normed, t)
            for g in range(HG):
                last = nc.tensor.transpose(self.o_bank[:, g * P:(g + 1) * P], m.o_t[:, b * HG + g, tb * P:(tb + 1) * P], m.ident[:, :])
            last.then_inc(self.o_turned, 1)
        elif kind == "on_turn":
            pe.wait_ge(self.o_normed, t + 1)
            wait(pe, self.on_copied, t)
            for k in range(CK):
                last = nc.tensor.transpose(self.n_bank[:, k * P:(k + 1) * P], self.o_norm[:, t % 2, k * P:(k + 1) * P], m.ident[:, :])
            last.then_inc(self.on_turned, 1)
        elif kind == "y_mm":
            if t == 0:
                pe.wait_ge(m.w_in[s["w_out_name"]], 16)
            pe.wait_ge(self.on_copied, t + 1)
            wait(pe, self.x_summed, t)
            for k in range(CK):
                last = nc.tensor.matmul(self.y_bank[:, 0:C], self.o_norm_t[:, t % 2, k, :], s["w_out"][b][:, k, :],
                                        start=(k == 0), stop=(k == CK - 1))
            last.then_inc(self.y_mm, 1)
        elif kind == "hat_turn":
            pe.wait_ge(self.hat_done, t + 1)
            if t % BLK == 0:
                wait(pe, self.h_done, CK * (t // BLK))
            for k in range(CK):
                last = nc.tensor.transpose(self.h_bank[k][:, (t % BLK) * P:(t % BLK + 1) * P], self.x_hat[:, t % 2, k * P:(k + 1) * P],
                                           m.ident[:, :])
            last.then_inc(self.hat_turned, 1)

    def vector_step(self, dve, chain, kind, t):
        nc, m, s = self.nc, self.m, self.s
        if kind == "o_norm":
            dve.wait_ge(self.o_turned, t + 1)
            wait(dve, self.on_turned, t - 1)
            heads = self.o_bank[:, :].rearrange("p (h e) -> p h e", e=HW)
            chain.link(nc.vector.reciprocal(self.recip[:, t % 2, :], heads[:, :, D:D + 1].rearrange("p h o -> p (h o)")))
            nc.vector.tensor_tensor(self.o_norm[:, t % 2, :].rearrange("p (h d) -> p h d", d=D), heads[:, :, 0:D],
                                    self.recip[:, t % 2, :].unsqueeze(2).to_broadcast([P, H, D]), ALU.mult).then_inc(self.o_normed, 1)
        elif kind == "x_sum":
            dve.wait_ge(self.y_mm, t + 1)
            dve.wait_ge(self.row_added, t + 1)
            nc.vector.tensor_tensor(m.x[:, t, :], m.x[:, t, :], self.y_bank[:, 0:C], ALU.add).then_inc(self.x_summed, 1)
        elif kind == "stats":
            if s["attended"]:
                dve.wait_ge(self.x_summed, t + 1)
            elif t == 0:
                dve.wait_ge(m.x_in, 16 * 3 * B)
            chain.link(nc.vector.bn_stats(self.stats[:, :], m.x[:, t, :]))
            nc.vector.bn_aggr(self.mean_var[:, t, :], self.stats[:, :]).then_inc(self.x_stats, 1)
            dve.wait_ge(self.x_stats, t + 1)
            dve.wait_ge(self.rstd_done, t + 1)
            wait(dve, self.hat_turned, t - 1)
            nc.vector.tensor_scalar(self.x_hat[:, t % 2, :], m.x[:, t, :], self.mean_var[:, t, 0:1], self.rstd[:, t:t + 1],
                                    ALU.subtract, ALU.mult).then_inc(self.hat_done, 1)

    def pool_step(self, pool, chain, kind, t):
        nc, s = self.nc, self.s
        if kind == "stats":
            pool.wait_ge(self.x_stats, t + 1)
            chain.link(nc.gpsimd.tensor_scalar(self.var_eps[:, t:t + 1], self.mean_var[:, t, 1:2], s["eps"], None, ALU.add))
            nc.gpsimd.tensor_tensor(self.rstd[:, t:t + 1], self.var_eps[:, t:t + 1], self.power[:, :], ALU.pow).then_inc(self.rstd_done, 1)

    def pool_rows(self, pool):
        for t in range(TILES):
            self.nc.gpsimd.tensor_tensor(self.m.x[:, t, :], self.m.x[:, t, :], self.m.res_row[:, self.s["row"], t // TB, :],
                                         ALU.add).then_inc(self.row_added, 1)

    def scalar_step(self, act, kind, t, h_free):
        nc, s = self.nc, self.s
        if kind == "on_copy":
            act.wait_ge(self.on_turned, t + 1)
            wait(act, self.y_mm, t - 1)
            nc.scalar.activation(self.o_norm_t[:, t % 2, :, :].rearrange("p k t -> p (k t)"), self.n_bank[:, 0:C], ACT.Copy).then_inc(self.on_copied, 1)
        elif kind == "modulate":
            act.wait_ge(self.hat_turned, BLK * (t + 1))
            h_free(act, t)
            scale, shift = s["modulate"](t * BLK // TB)
            for k in range(CK):
                nc.scalar.activation(self.h_t[:, t % 2, k, :], self.h_bank[k][:, :], ACT.Identity, bias=shift[:, k:k + 1],
                                     scale=scale[:, k:k + 1]).then_inc(self.h_done, 1)


def projection_stage(nc, m, name, spec):
    with ExitStack() as ctx:
        st = TokenStage(nc, m, ctx, name, spec)
        parts = st.sb("parts", [P, 2, 3, BT], BF16)
        full = st.sb("full", [P, 2, BT])
        rest = st.sb("rest", [P, BT])
        qk_units = spec["qk"]
        NQ = len(qk_units)
        has_v = spec["v"] is not None
        if has_v:
            v_out = st.sb("v_out", [P, 2, H, HW])
        qk_mm, qk_full, qk_hi, qk_rest, qk_parts, v_mm, v_done, v_ones = (
            st.sem(n) for n in ("qk_mm", "qk_full", "qk_hi", "qk_rest", "qk_parts", "v_mm", "v_done", "v_ones"))
        part_stored = [st.sem(f"part_stored{i}") for i in range(2)]
        v_stored = [st.sem(f"v_stored{i}") for i in range(2)]

        def projections(block):
            out = [("qk", block * NQ + u) for u in range(NQ)]
            if has_v:
                out += [("v", block * BLK + t) for t in range(BLK)]
            return out

        plan = st.attention_steps(0)
        for n in range(NB):
            ahead = st.attention_steps(n + 1) if n + 1 < NB else []
            plan += interleave(projections(n), ahead) if len(ahead) <= NQ else interleave(ahead, projections(n))

        def h_free(act, n):
            if has_v:
                wait(act, v_mm, BLK * (n - 1))
            else:
                wait(act, qk_mm, NQ * (n - 1))

        with nc.Block() as block:

            @block.tensor
            def _(pe):
                pe.wait_ge(m.ident_in, 1)
                for kind, i in plan:
                    if kind == "qk":
                        n, u = i // NQ, i % NQ
                        w, col, _, _, _, _ = qk_units[u]
                        if i == 0:
                            pe.wait_ge(m.w_in[spec["w_name"]], 16)
                            for other in spec["w_more"]:
                                pe.wait_ge(m.w_in[other], 16)
                        pe.wait_ge(st.h_done, CK * (n + 1))
                        wait(pe, qk_hi, i - 1)
                        for k in range(CK):
                            last = nc.tensor.matmul(st.p_bank[i % 2][:, :], w[:, k, col:col + P], st.h_t[:, n % 2, k, :],
                                                    start=(k == 0), stop=(k == CK - 1))
                        last.then_inc(qk_mm, 1)
                    elif kind == "v":
                        w, col = spec["v"]
                        wait(pe, v_done, i)
                        for k in range(CK):
                            last = nc.tensor.matmul(st.p_bank[2][:, 0:C], st.h_t[:, (i // BLK) % 2, k, (i % BLK) * P:(i % BLK + 1) * P],
                                                    w[:, k, col:col + C], start=(k == 0), stop=(k == CK - 1))
                        last.then_inc(v_mm, 1)
                    else:
                        st.tensor_step(pe, kind, i)

            @block.scalar
            def _(act):
                for kind, i in plan:
                    if kind == "qk":
                        _, _, bias, scale, _, _ = qk_units[i % NQ]
                        act.wait_ge(qk_mm, i + 1)
                        wait(act, qk_rest, i - 1)
                        nc.scalar.activation(full[:, i % 2, :], st.p_bank[i % 2][:, :], ACT.Identity, bias=bias, scale=scale).then_inc(qk_full, 1)
                        wait(act, part_stored[i % 2], 16 * (i // 2))
                        nc.scalar.activation(parts[:, i % 2, 0, :], st.p_bank[i % 2][:, :], ACT.Identity, bias=bias, scale=scale).then_inc(qk_hi, 1)
                    else:
                        st.scalar_step(act, kind, i, h_free)

            @block.vector
            def _(dve):
                chain = Chain(dve, st.dve_chain)
                for kind, i in plan:
                    if kind == "qk":
                        dve.wait_ge(qk_full, i + 1)
                        dve.wait_ge(qk_hi, i + 1)
                        wait(dve, qk_parts, i)
                        nc.vector.tensor_tensor(rest[:, :], full[:, i % 2, :], parts[:, i % 2, 0, :], ALU.subtract).then_inc(qk_rest, 1)
                        dve.wait_ge(qk_rest, i + 1)
                        chain.link(nc.vector.tensor_copy(parts[:, i % 2, 1, :], rest[:, :]))
                        nc.vector.tensor_tensor(parts[:, i % 2, 2, :], rest[:, :], parts[:, i % 2, 1, :], ALU.subtract).then_inc(qk_parts, 1)
                    elif kind == "v":
                        dve.wait_ge(v_mm, i + 1)
                        if i == 0:
                            dve.wait_ge(v_ones, 1)
                        wait(dve, v_stored[i % 2], 16 * (i // 2))
                        nc.vector.tensor_tensor(v_out[:, i % 2, :, 0:D], st.p_bank[2][:, 0:C].rearrange("p (h d) -> p h d", d=D),
                                                spec["v_row"].rearrange("p (h d) -> p h d", d=D), ALU.add).then_inc(v_done, 1)
                    else:
                        st.vector_step(dve, chain, kind, i)

            @block.gpsimd
            def _(pool):
                chain = Chain(pool, st.pool_chain)
                chain.link(nc.gpsimd.memset(st.power[:, :], -0.5))
                if has_v:
                    nc.gpsimd.memset(v_out[:, :, :, D:HW], 1.0).then_inc(v_ones, 1)
                if spec["attended"]:
                    st.pool_rows(pool)
                for kind, i in plan:
                    st.pool_step(pool, chain, kind, i)

            @block.sync
            def _(sp):
                for kind, i in plan:
                    if kind == "qk":
                        n = i // NQ
                        _, _, _, _, dest, half = qk_units[i % NQ]
                        b, t0 = n * BT // L, n * BT % L
                        sp.wait_ge(qk_parts, i + 1)
                        sp.dma_start(dest[:, b * C + half * P:b * C + (half + 1) * P, t0:t0 + BT].rearrange("s r t -> r s t"),
                                     parts[:, i % 2, :, :]).then_inc(part_stored[i % 2], 16)
                    elif kind == "v":
                        b, t = i // TB, i % TB
                        sp.wait_ge(v_done, i + 1)
                        sp.dma_start(m.v_dram[b * HG:(b + 1) * HG, t * P:(t + 1) * P, :].rearrange("g p e -> p g e"),
                                     v_out[:, i % 2, :, :].rearrange("p (g h) e -> p g (h e)", g=HG)).then_inc(v_stored[i % 2], 16)
                for i in range(2):
                    sp.wait_ge(part_stored[i], 16 * NQ * NB // 2)
                    if has_v:
                        sp.wait_ge(v_stored[i], 16 * TILES // 2)


def mlp_stage(nc, m, name, spec):
    with ExitStack() as ctx:
        st = TokenStage(nc, m, ctx, name, spec)
        HT = HID // P
        gated = spec["gated"]
        hidden = st.sb("hidden", [P, 2, HT, BT])
        if gated:
            silu = st.sb("silu", [P, 2, BT])
        a_mm, b_mm, act_done, hid_done, down_mm, out_sum, row2_added = (
            st.sem(n) for n in ("a_mm", "b_mm", "act_done", "hid_done", "down_mm", "out_sum", "row2_added"))
        stored = st.sem("stored")
        w_up, w_down, b_up = spec["w_up"], spec["w_down"], spec["b_up"]

        def mlp(block):
            return [("up", block * HT + j) for j in range(HT)] + [("down", block * BLK + t) for t in range(BLK)]

        plan = st.attention_steps(0)
        for n in range(NB):
            ahead = st.attention_steps(n + 1) if n + 1 < NB else []
            plan += interleave(mlp(n), ahead) if len(ahead) <= HT else interleave(ahead, mlp(n))

        def h_free(act, n):
            wait(act, b_mm if gated else a_mm, HT * (n - 1))

        with nc.Block() as block:

            @block.tensor
            def _(pe):
                pe.wait_ge(m.ident_in, 1)
                for kind, i in plan:
                    if kind == "up":
                        n, j = i // HT, i % HT
                        if i == 0:
                            pe.wait_ge(m.w_in[spec["up_name"]], 16)
                        pe.wait_ge(st.h_done, CK * (n + 1))
                        wait(pe, act_done, i if gated else i - 1)
                        bank = st.p_bank[0] if gated else st.p_bank[i % 2]
                        for k in range(CK):
                            last = nc.tensor.matmul(bank[:, :], w_up[:, k, j * P:(j + 1) * P], st.h_t[:, n % 2, k, :],
                                                    start=(k == 0), stop=(k == CK - 1))
                        last.then_inc(a_mm, 1)
                        if gated:
                            wait(pe, hid_done, i)
                            for k in range(CK):
                                last = nc.tensor.matmul(st.p_bank[1][:, :], w_up[:, k, HID + j * P:HID + (j + 1) * P], st.h_t[:, n % 2, k, :],
                                                        start=(k == 0), stop=(k == CK - 1))
                            last.then_inc(b_mm, 1)
                    elif kind == "down":
                        n, t = i // BLK, i % BLK
                        if i == 0:
                            pe.wait_ge(m.w_in[spec["down_name"]], 16)
                        pe.wait_ge(hid_done if gated else act_done, HT * (n + 1))
                        wait(pe, out_sum, i)
                        for j in range(HT):
                            last = nc.tensor.matmul(st.p_bank[2][:, 0:C], hidden[:, n % 2, j, t * P:(t + 1) * P], w_down[i // TB][:, j, :],
                                                    start=(j == 0), stop=(j == HT - 1))
                        last.then_inc(down_mm, 1)
                    else:
                        st.tensor_step(pe, kind, i)

            @block.scalar
            def _(act):
                for kind, i in plan:
                    if kind == "up":
                        n, j = i // HT, i % HT
                        act.wait_ge(a_mm, i + 1)
                        if gated:
                            wait(act, hid_done, i - 1)
                            nc.scalar.activation(silu[:, i % 2, :], st.p_bank[0][:, :], ACT.Silu, bias=b_up[:, j:j + 1]).then_inc(act_done, 1)
                        else:
                            if j == 0:
                                wait(act, down_mm, BLK * (n - 1))
                            nc.scalar.activation(hidden[:, n % 2, j, :], st.p_bank[i % 2][:, :], ACT.Gelu, bias=b_up[:, j:j + 1]).then_inc(act_done, 1)
                    elif kind != "down":
                        st.scalar_step(act, kind, i, h_free)

            @block.vector
            def _(dve):
                chain = Chain(dve, st.dve_chain)
                for kind, i in plan:
                    if kind == "up":
                        if gated:
                            n, j = i // HT, i % HT
                            dve.wait_ge(act_done, i + 1)
                            dve.wait_ge(b_mm, i + 1)
                            if j == 0:
                                wait(dve, down_mm, BLK * (n - 1))
                            nc.vector.scalar_tensor_tensor(hidden[:, n % 2, j, :], st.p_bank[1][:, :], b_up[:, HT + j:HT + j + 1],
                                                           silu[:, i % 2, :], ALU.add, ALU.mult).then_inc(hid_done, 1)
                    elif kind == "down":
                        dve.wait_ge(down_mm, i + 1)
                        dve.wait_ge(row2_added, i + 1)
                        nc.vector.tensor_tensor(m.x[:, i, :], m.x[:, i, :], st.p_bank[2][:, 0:C], ALU.add).then_inc(out_sum, 1)
                    else:
                        st.vector_step(dve, chain, kind, i)

            @block.gpsimd
            def _(pool):
                chain = Chain(pool, st.pool_chain)
                chain.link(nc.gpsimd.memset(st.power[:, :], -0.5))
                st.pool_rows(pool)
                for kind, i in plan:
                    if kind == "down":
                        pool.wait_ge(st.hat_done, i + 1)
                        nc.gpsimd.tensor_tensor(m.x[:, i, :], m.x[:, i, :], m.res_row[:, spec["row"] + 1, i // TB, :], ALU.add).then_inc(row2_added, 1)
                    else:
                        st.pool_step(pool, chain, kind, i)

            @block.sync
            def _(sp):
                if spec["out"] is None:
                    return
                count = 0
                for t in range(TILES):
                    b, tb = t // TB, t % TB
                    sp.wait_ge(out_sum, t + 1)
                    t0 = SHIFT + tb * P
                    if t0 + P <= L:
                        sp.dma_start(spec["out"][b, t0:t0 + P, :], m.x[:, t, :]).then_inc(stored, 16)
                        count += 1
                    else:
                        sp.dma_start(spec["out"][b, t0:L, :], m.x[0:L - t0, t, :]).then_inc(stored, 16)
                        sp.dma_start(spec["out"][b, 0:P - (L - t0), :], m.x[L - t0:P, t, :]).then_inc(stored, 16)
                        count += 2
                sp.wait_ge(stored, 16 * count)



def short_attention_stage(nc, m, name, kind):
    window, topk, masked = kind == "window", kind == "topk", kind == "masked"
    NK = P if window else S2
    QR = PACK + 1 if masked else PACK
    with ExitStack() as ctx:
        sb = lambda n, shape, dt=F32: ctx.enter_context(nc.sbuf_tensor(name + n, shape, dt))
        sem = stage_semaphores(nc, ctx, name)
        SW = P if window else C
        PW = S2 if masked else P
        KT = L if window else S2
        VT = TB if window else 1
        qs = sb("qs", [PACK + 1, 2, HG, L], BF16)
        ks = sb("ks", [PACK + 1, 2, HG, KT], BF16)
        vs = sb("vs", [P, 2, VT, HG * HW])
        probs = sb("probs", [P, 2, HG, PW])
        neg_max = sb("neg_max", [P, 2, HG])
        probs_t = sb("probs_t", [P, HG * P + P])
        if topk:
            top = sb("top", [P, 2, HG, TOPK])
            left1 = sb("left1", [P, HG, S2])
            left2 = sb("left2", [P, 2, HG, S2])
            exp_all = sb("exp_all", [P, 2, HG, S2])
            exp_left = sb("exp_left", [P, 2, HG, S2])
        if not window:
            vt = sb("vt", [P, 2, HG * HW])
            tails = sb("tails", [P, 2, HG, HW])
        s_bank = [ctx.enter_context(nc.psum_tensor(name + f"s_bank{i}", [P, HG, SW], F32)) for i in range(2)]
        t_bank = ctx.enter_context(nc.psum_tensor(name + "t_bank", [P, HG * P], F32))
        tail_bank = ctx.enter_context(nc.psum_tensor(name + "tail_bank", [P, 512], F32))
        o_bank = [ctx.enter_context(nc.psum_tensor(name + f"o_bank{i}", [P, BT], F32)) for i in range(2)]
        group_in = [sem(f"group_in{i}") for i in range(2)]
        scores, max_done, exp_done, turned, copied, pv_done, o_copied, zeroed = (
            sem(n) for n in ("scores", "max_done", "exp_done", "turned", "copied", "pv_done", "o_copied", "zeroed"))
        picked, left_done, diff_done, passed = (sem(n) for n in ("picked", "left_done", "diff_done", "passed"))
        q_dram = m.q_dram
        k_dram = m.k_dram if window else m.ctx_k[1 if masked else 0]
        v_dram = m.v_dram if window else m.ctx_v[1 if masked else 0]
        FILLS = 0 if window else 3 if masked else 2
        LOADS = 2 * len(Q_PART) + (1 if window else 1 + HG + (1 if masked else 0))

        def load_group(sp, n, j):
            rows = lambda dram, part, length: dram[part, ds(n * HG * D, HG * D), 0:length].rearrange("(h d) t -> d h t", d=D)
            for r in range(len(Q_PART)):
                sp.dma_start(qs[r * D:(r + 1) * D, j, :, :], rows(q_dram, Q_PART[r], L)).then_inc(group_in[j], 16)
                sp.dma_start(ks[r * D:(r + 1) * D, j, :, :], rows(k_dram, K_PART[r], KT)).then_inc(group_in[j], 16)
            v = v_dram[ds(n, 1), :, :].rearrange("o t e -> (o t) e")
            if window:
                sp.dma_start(vs[:, j, :, :], v.rearrange("(k p) e -> p k e", p=P)).then_inc(group_in[j], 16)
            else:
                sp.dma_start(vs[:, j, 0, :], v[0:P, :]).then_inc(group_in[j], 16)
                for h in range(HG):
                    sp.dma_start(vt[h * HW:h * HW + TAIL, j, h * HW:(h + 1) * HW], v[P:S2, h * HW:(h + 1) * HW]).then_inc(group_in[j], 16)
            if masked:
                sp.dma_start(ks[PACK:PACK + 1, j, :, :], m.ctx_mask[ds(n, 1), :, :]).then_inc(group_in[j], 16)

        def arrived(n, j):
            return 16 * LOADS * ((n - j) // 2 + 1) if isinstance(n, int) else (n - j) * (8 * LOADS) + 16 * LOADS

        with nc.Block() as block:

            @block.sync
            def _(sp):
                wait(sp, zeroed, FILLS)
                load_group(sp, 0, 0)
                load_group(sp, 1, 1)
                with sp.Fori(0, (G - 2) // 2, 1) as i:
                    for j in range(2):
                        n = i * 2 + (2 + j)
                        sp.wait_ge(pv_done, (n - 1) * TB)
                        load_group(sp, n, j)

            @block.gpsimd
            def _(pool):
                fills = Chain(pool, zeroed)
                if not window:
                    fills.link(nc.gpsimd.memset(vt[:, :, :], 0.0))
                    fills.link(nc.gpsimd.memset(tails[:, :, :, :], 0.0))
                if masked:
                    fills.link(nc.gpsimd.memset(qs[PACK:PACK + 1, :, :, :], 1.0))
                if masked:
                    def body(n, j, first, last):
                        for t in range(TB):
                            wait_apart(pool, exp_done, n * TB + (t + 1), passed)
                            nc.gpsimd.tensor_copy(tails[:, t % 2, :, 0:TAIL], probs[:, t % 2, :, P:S2]).then_inc(diff_done, 1)
                    each_group(pool, 2, body)
                if topk:
                    def body(n, j, first, last):
                        for t in range(TB):
                            u, s = n * TB + t, t % 2
                            for half in range(2):
                                pool.wait_ge(exp_done, u * 2 + (half + 1))
                                hh = slice(2 * half, 2 * half + 2)
                                nc.gpsimd.tensor_tensor(tails[:, s, hh, 0:TAIL], exp_all[:, s, hh, P:S2], exp_left[:, s, hh, P:S2], ALU.subtract)
                                nc.gpsimd.tensor_tensor(probs[:, s, hh, :], exp_all[:, s, hh, 0:P], exp_left[:, s, hh, 0:P],
                                                        ALU.subtract).then_inc(diff_done, 1)
                    each_group(pool, 2, body)

            @block.tensor
            def _(pe):
                pe.wait_ge(m.ident_in, 1)
                wait(pe, zeroed, FILLS)

                def score(n, j, t):
                    u = n * TB + t
                    if t == 0:
                        pe.wait_ge(group_in[j], arrived(n, j))
                    wait(pe, exp_done, (u - 1) * (2 if topk else 1))
                    for h in range(HG):
                        k0 = t * P if window else 0
                        last = nc.tensor.matmul(s_bank[t % 2][:, h, 0:NK], qs[0:QR, j, h, t * P:(t + 1) * P], ks[0:QR, j, h, k0:k0 + NK],
                                                start=True, stop=True)
                    last.then_inc(scores, 1)

                def body(n, j, first, last_group):
                    if first:
                        score(0, 0, 0)
                        score(0, 0, 1)
                    for t in range(TB):
                        u = n * TB + t
                        wait(pe, copied, u)
                        for h in range(HG):
                            if topk:
                                if h % 2 == 0:
                                    pe.wait_ge(diff_done, u * 2 + (h // 2 + 1))
                            elif h == 0:
                                pe.wait_ge(exp_done, u + 1)
                            last = nc.tensor.transpose(t_bank[:, h * P:(h + 1) * P], probs[:, t % 2, h, 0:P], m.ident[:, :])
                        if not window:
                            if masked:
                                pe.wait_ge(diff_done, u + 1)
                            last = nc.tensor.transpose(tail_bank[:, 0:P], tails[:, t % 2, :, :].rearrange("p h e -> p (h e)"), m.ident[:, :])
                        last.then_inc(turned, 1)
                        if t + 2 < TB:
                            score(n, j, t + 2)
                        elif not last_group:
                            score(n + 1, 1 - j, t + 2 - TB)
                        pe.wait_ge(copied, u + 1)
                        if t % BLK == 0:
                            wait(pe, o_copied, n * 2 + (t // BLK - 1))
                        out = o_bank[t // BLK][:, (t % BLK) * P:(t % BLK + 1) * P]
                        if not window:
                            nc.tensor.matmul(out, vt[:, j, :], probs_t[:, HG * P:HG * P + P], start=True, stop=False, skip_group_check=True)
                        for h in range(HG):
                            last = nc.tensor.matmul(out[h * HW:(h + 1) * HW, :], vs[:, j, t if window else 0, h * HW:(h + 1) * HW],
                                                    probs_t[:, h * P:(h + 1) * P], start=window, stop=True, skip_group_check=True)
                        last.then_inc(pv_done, 1)

                each_group(pe, 2, body)

            def copy_transposes(eng, u):
                eng.wait_ge(turned, u + 1)
                if eng is nc.vector:
                    if not window:
                        nc.vector.tensor_copy(probs_t[:, HG * P:HG * P + P], tail_bank[:, 0:P])
                    nc.vector.tensor_copy(probs_t[:, 0:HG * P], t_bank[:, :]).then_inc(copied, 1)
                else:
                    nc.scalar.activation(probs_t[:, HG * P:HG * P + P], tail_bank[:, 0:P], ACT.Copy)
                    nc.scalar.activation(probs_t[:, 0:HG * P], t_bank[:, :], ACT.Copy).then_inc(copied, 1)

            @block.vector
            def _(dve):
                def maxima(u, s):
                    dve.wait_ge(scores, u + 1)
                    nc.vector.tensor_reduce(neg_max[:, s, :], s_bank[s][:, :, 0:NK], axis=AX.X, op=ALU.max, negate=True).then_inc(max_done, 1)

                def top16(u, s):
                    wait_apart(dve, scores, u + 1, passed)
                    for h in range(HG):
                        nc.vector.max(top[:, s, h, 0:8], s_bank[s][:, h, 0:S2]).then_inc(picked, 1)
                    dve.wait_ge(picked, u * 12 + 4)
                    nc.vector.tensor_scalar(neg_max[:, s, :], top[:, s, :, 0], -1.0, None, ALU.mult)
                    for h in range(HG):
                        nc.vector.match_replace(left1[:, h, :], top[:, s, h, 0:8], s_bank[s][:, h, 0:S2], -FAR).then_inc(picked, 1)
                    wait_apart(dve, picked, u * 12 + 8, passed)
                    for h in range(HG):
                        nc.vector.max(top[:, s, h, 8:16], left1[:, h, :]).then_inc(picked, 1)
                    wait_apart(dve, picked, u * 12 + 12, passed)
                    for h in range(HG):
                        nc.vector.match_replace(left2[:, s, h, :], top[:, s, h, 8:16], left1[:, h, :], -FAR).then_inc(left_done, 1)

                def body(n, j, first, last):
                    if topk:
                        for t in range(TB):
                            top16(n * TB + t, t % 2)
                        return
                    if first:
                        maxima(0, 0)
                    for t in range(TB):
                        u = n * TB + t
                        if not (last and t == TB - 1):
                            maxima(u + 1, (t + 1) % 2)
                        copy_transposes(nc.vector, u)

                each_group(dve, 2, body)

            @block.scalar
            def _(act):
                def copy_output(n, half):
                    act.wait_ge(pv_done, n * TB + (half + 1) * BLK)
                    out = m.o_t[:, ds(n, 1), half * BT:(half + 1) * BT].rearrange("p o t -> p (o t)")
                    nc.scalar.activation(out, o_bank[half][:, :], ACT.Copy).then_inc(o_copied, 1)

                def exp_scores(u, s, out, src, sem_):
                    for h in range(HG):
                        e = nc.scalar.activation(out[:, s, h, 0:NK], src[:, h, 0:NK], ACT.Exp, bias=neg_max[:, s, h:h + 1])
                        if sem_ is not None and h == HG - 1:
                            e.then_inc(sem_, 1)

                def body(n, j, first, last):
                    if topk and first:
                        act.wait_ge(picked, 8)
                        exp_scores(0, 0, exp_all, s_bank[0], None)
                    for t in range(TB):
                        u, s = n * TB + t, t % 2
                        if topk:
                            for h in range(HG):
                                if h % 2 == 0:
                                    act.wait_ge(left_done, u * 4 + (h + 2))
                                e = nc.scalar.activation(exp_left[:, s, h, :], left2[:, s, h, :], ACT.Exp, bias=neg_max[:, s, h:h + 1])
                                if h % 2 == 1:
                                    e.then_inc(exp_done, 1)
                            if not (last and t == TB - 1):
                                act.wait_ge(picked, u * 12 + 20)
                                exp_scores(u + 1, 1 - s, exp_all, s_bank[1 - s], None)
                            copy_transposes(nc.scalar, u)
                        else:
                            act.wait_ge(max_done, u + 1)
                            exp_scores(u, s, probs, s_bank[s], exp_done)
                        if t == BLK + 1:
                            copy_output(n, 0)
                        if t == 1 and not first:
                            copy_output(n - 1, 1)
                    if last:
                        copy_output(n, 1)

                each_group(act, 2, body)



def full_attention_stage(nc, m, name):
    QC = L // 512
    STEPS = QC * TB
    NM = HG * TB * QC
    FULL = PACK + 3
    with ExitStack() as ctx:
        sb = lambda n, shape, dt=F32: ctx.enter_context(nc.sbuf_tensor(name + n, shape, dt))
        sem = stage_semaphores(nc, ctx, name)
        qs = sb("qs", [FULL, 3, HG, L], BF16)
        ks = sb("ks", [FULL, 3, HG, L], BF16)
        vs = sb("vs", [P, 3, TB, HG * HW])
        probs = sb("probs", [P, 2, 2, 2, 512])
        part_max = sb("part_max", [P, HG * TB, QC])
        neg_max = sb("neg_max", [P, HG * TB])
        max_rest = sb("max_rest", [HG * TB, P])
        max_parts = sb("max_parts", [HG * TB, 3, P], BF16)
        s_bank = [ctx.enter_context(nc.psum_tensor(name + f"s_bank{i}", [P, 2, 512], F32)) for i in range(2)]
        m_bank = [ctx.enter_context(nc.psum_tensor(name + f"m_bank{i}", [P, 512], F32)) for i in range(2)]
        o_bank = ctx.enter_context(nc.psum_tensor(name + "o_bank", [P, 512], F32))
        r_bank = ctx.enter_context(nc.psum_tensor(name + "r_bank", [P, 512], F32))
        group_in = [sem(f"group_in{i}") for i in range(3)]
        max_in = [sem(f"max_in{i}") for i in range(3)]
        ones_set, max_mm, max_read, max_all, max_turned, max_split, chain_sem = (
            sem(n) for n in ("ones_set", "max_mm", "max_read", "max_all", "max_turned", "max_split", "chain"))
        scores, exp_done, pv_done, o_copied = (sem(n) for n in ("scores", "exp_done", "pv_done", "o_copied"))
        LOADS = 2 * len(Q_PART) + 1
        PER = [5] * 12 + [4] + [0] * 3
        assert sum(PER) == NM and len(PER) == STEPS

        def per3(n, j):
            return lambda by, plus: ((n - j) // 3) * by + plus

        with nc.Block() as block:

            @block.gpsimd
            def _(pool):
                nc.gpsimd.memset(ks[PACK:FULL, :, :, :], 1.0).then_inc(ones_set, 1)

            @block.sync
            def _(sp):
                def load_group(n, j):
                    rows = lambda dram, part: dram[part, ds(n * HG * D, HG * D), :].rearrange("(h d) t -> d h t", d=D)
                    for r in range(len(Q_PART)):
                        sp.dma_start(qs[r * D:(r + 1) * D, j, :, :], rows(m.q_dram, Q_PART[r])).then_inc(group_in[j], 16)
                        sp.dma_start(ks[r * D:(r + 1) * D, j, :, :], rows(m.k_dram, K_PART[r])).then_inc(group_in[j], 16)
                    v = m.v_dram[ds(n, 1), :, :].rearrange("o (k p) e -> p (o k) e", p=P)
                    sp.dma_start(vs[:, j, :, :], v).then_inc(group_in[j], 16)

                def maxima_rows(n, j):
                    sp.wait_ge(max_split, n * 3 + 3)
                    for part in range(3):
                        sp.dma_start(qs[PACK + part:PACK + part + 1, j, :, :].rearrange("o h t -> o (h t)"),
                                     max_parts[:, part, :]).then_inc(max_in[j], 16)

                load_group(0, 0)
                load_group(1, 1)
                maxima_rows(0, 0)
                load_group(2, 2)

                def body(n, j, first, last):
                    if last:
                        return
                    maxima_rows(n + 1, (j + 1) % 3)
                with_loads = lambda n: None
                del with_loads
                body(0, 0, True, False)
                with sp.Fori(0, 1, 1) as i:
                    for j in range(3):
                        n = i * 3 + (j + 1)
                        sp.wait_ge(pv_done, n * STEPS)
                        load_group(n + 2, j % 3)
                        maxima_rows(n + 1, (j + 2) % 3)
                for n in (4, 5):
                    sp.wait_ge(pv_done, n * STEPS)
                    load_group(n + 2, (n + 2) % 3)
                    maxima_rows(n + 1, (n + 1) % 3)
                maxima_rows(7, 1)

            @block.tensor
            def _(pe):
                pe.wait_ge(m.ident_in, 1)
                pe.wait_ge(ones_set, 1)

                def max_block(n, j, i):
                    h, t, kc = i // (TB * QC), i // QC % TB, i % QC
                    wait(pe, max_read, n * NM + (i - 1))
                    nc.tensor.matmul(m_bank[i % 2][:, :], qs[0:PACK, j, h, t * P:(t + 1) * P], ks[0:PACK, j, h, kc * 512:(kc + 1) * 512],
                                     start=True, stop=True).then_inc(max_mm, 1)

                def turn_maxima(n):
                    pe.wait_ge(max_all, n + 1)
                    nc.tensor.transpose(r_bank[0:HG * TB, 0:P], neg_max[:, :], m.ident[:, :]).then_inc(max_turned, 1)

                def weigh(n, j, d):
                    u = n * STEPS + d
                    pe.wait_ge(exp_done, u * 2 + 2)
                    if d % TB == 0:
                        wait(pe, o_copied, n * QC + d // TB)
                    for h in range(HG):
                        last = nc.tensor.matmul(o_bank[h * HW:(h + 1) * HW, :], vs[:, j, d % TB, h * HW:(h + 1) * HW],
                                                probs[:, d % 2, h // 2, h % 2, :], start=(d % TB == 0), stop=(d % TB == TB - 1),
                                                skip_group_check=True)
                    last.then_inc(pv_done, 1)

                def body(n, j, first, last):
                    if first:
                        pe.wait_ge(group_in[0], 16 * LOADS)
                        for i in range(NM):
                            max_block(0, 0, i)
                        turn_maxima(0)
                    if not last:
                        j1 = (j + 1) % 3
                        wait(pe, group_in[j1], per3(n + 1, j1)(16 * LOADS, 16 * LOADS) if isinstance(n, int)
                             else group_value(n + 1, j1, 16 * LOADS))
                    wait(pe, max_in[j], per3(n, j)(48, 48) if isinstance(n, int) else group_value(n, j, 48))
                    i = 0
                    for d in range(STEPS):
                        qc, kt = d // TB, d % TB
                        u = n * STEPS + d
                        for pair in range(2):
                            wait(pe, exp_done, u * 2 + (pair - 1))
                            for h in range(2):
                                mm = nc.tensor.matmul(s_bank[pair][:, h, :], ks[0:FULL, j, 2 * pair + h, kt * P:(kt + 1) * P],
                                                      qs[0:FULL, j, 2 * pair + h, qc * 512:(qc + 1) * 512], start=True, stop=True)
                            mm.then_inc(scores, 1)
                        if not last:
                            for _ in range(PER[d]):
                                max_block(n + 1, j1, i)
                                i += 1
                        if d > 0:
                            weigh(n, j, d - 1)
                        elif not first:
                            weigh(n - 1, (j - 1) % 3, STEPS - 1)
                        if not last and d == STEPS - 2:
                            turn_maxima(n + 1)
                    if last:
                        weigh(n, j, STEPS - 1)

                def group_value(n, j, by):
                    return (n - j) * (by // 3 if by % 3 == 0 else 0) + by

                each_group(pe, 3, body)

            @block.vector
            def _(dve):
                def reduce(n, i):
                    dve.wait_ge(max_mm, n * NM + (i + 1))
                    nc.vector.tensor_reduce(part_max[:, i // QC, i % QC:i % QC + 1], m_bank[i % 2][:, :], axis=AX.X, op=ALU.max).then_inc(max_read, 1)

                def group_maxima(n, waits):
                    for i in range(NM):
                        reduce(n, i)
                    dve.wait_ge(max_read, n * NM + NM)
                    nc.vector.tensor_reduce(neg_max[:, :], part_max[:, :, :], axis=AX.X, op=ALU.max, negate=True).then_inc(max_all, 1)
                    dve.wait_ge(max_turned, n + 1)
                    turned = r_bank[0:HG * TB, 0:P]
                    if waits is not None:
                        dve.wait_ge(*waits)
                    nc.vector.tensor_copy(max_parts[:, 0, :], turned).then_inc(max_split, 1)
                    dve.wait_ge(max_split, n * 3 + 1)
                    nc.vector.tensor_tensor(max_rest[:, :], turned, max_parts[:, 0, :], ALU.subtract).then_inc(chain_sem, 1)
                    dve.wait_ge(chain_sem, n + 1)
                    nc.vector.tensor_copy(max_parts[:, 1, :], max_rest[:, :]).then_inc(max_split, 1)
                    dve.wait_ge(max_split, n * 3 + 2)
                    nc.vector.tensor_tensor(max_parts[:, 2, :], max_rest[:, :], max_parts[:, 1, :], ALU.subtract).then_inc(max_split, 1)

                def body(n, j, first, last):
                    if first:
                        group_maxima(0, None)
                    if not last:
                        value = (n - j) * 16 + 48
                        group_maxima(n + 1, (max_in[j], value))

                each_group(dve, 3, body)

            @block.scalar
            def _(act):
                def copy_output(n, qc):
                    act.wait_ge(pv_done, n * STEPS + (qc + 1) * TB)
                    out = m.o_t[:, ds(n, 1), qc * 512:(qc + 1) * 512].rearrange("p o t -> p (o t)")
                    nc.scalar.activation(out, o_bank[:, :], ACT.Copy).then_inc(o_copied, 1)

                def body(n, j, first, last):
                    for d in range(STEPS):
                        u = n * STEPS + d
                        for pair in range(2):
                            act.wait_ge(scores, u * 2 + (pair + 1))
                            nc.scalar.activation(probs[:, d % 2, pair, :, :], s_bank[pair][:, :, :], ACT.Exp).then_inc(exp_done, 1)
                        if d == TB:
                            copy_output(n, 0)
                        if d == 0 and not first:
                            copy_output(n - 1, 1)
                    if last:
                        copy_output(n, 1)

                each_group(act, 3, body)



def build(nc, a, out):
    L0, L1 = "L0_xcond_", "L1_xcond_"
    m = Memory()
    m.q_dram = nc.dram_tensor("q_dram", (3, B * C, L), BF16).ap()
    m.k_dram = nc.dram_tensor("k_dram", (3, B * C, L), BF16).ap()
    m.v_dram = nc.dram_tensor("v_dram", (G, L, HG * HW), F32).ap()
    m.ctx_k = [nc.dram_tensor(f"ctx_k{x}", (3, B * C, S2), BF16).ap() for x in range(2)]
    m.ctx_v = [nc.dram_tensor(f"ctx_v{x}", (G, S2, HG * HW), F32).ap() for x in range(2)]
    m.ctx_mask = nc.dram_tensor("ctx_mask", (G, HG, S2), BF16).ap()
    with ExitStack() as ctx:
        sb = lambda name, shape, dt=F32: ctx.enter_context(nc.sbuf_tensor(name, shape, dt))
        sem = lambda name: ctx.enter_context(nc.semaphore(name))
        m.x = sb("x_sb", [P, TILES, C])
        m.o_t = sb("o_t", [P, G, L])
        m.ident = sb("ident", [P, P])
        m.mod = sb("mod", [P, 18, B])
        m.res_row = sb("res_row", [P, 6, B, C])
        m.x_in, m.ident_in = sem("x_in"), sem("ident_in")
        w = {}
        order = [(L0 + "w_kv", 2 * C), (L1 + "ca_wk", C), (L1 + "ca_wv", C), (L0 + "w_qkv", 3 * C), (L0 + "w_so", C), (L0 + "w_q", C),
                 (L0 + "w_co", C), (L1 + "sa_wq", C), (L1 + "sa_wk", C), (L1 + "sa_wv", C), (L1 + "sa_wo", C), (L1 + "ca_wq", C), (L1 + "ca_wo", C)]
        for name, n in order:
            w[name] = sb("w_" + name, [P, CK, n])
        w_so2, w_co2 = sb("w_so2", [P, CK, C]), sb("w_co2", [P, CK, C])
        m.columns = sb("columns", [P, sum(n for _, n in COLUMNS)])
        col, at = {}, 0
        for name, n in COLUMNS:
            col[name] = m.columns[:, at:at + n]
            at += n
        m.ada_col = col[L0 + "b_ada"]
        m.query_columns = [col[L0 + "b_qkv"][:, 0:CK], col[L0 + "b_q"][:, :], col[L1 + "sa_bq"][:, :], col[L1 + "ca_bq"][:, :]]
        v_rows = [sb(f"v_row{i}", [P, C]) for i in range(4)]
        m.value_rows = [(v_rows[0][:, :], a[L0 + "b_qkv"][2 * C:3 * C]), (v_rows[1][:, :], a[L0 + "b_kv"][C:2 * C]),
                        (v_rows[2][:, :], a[L1 + "sa_bv"]), (v_rows[3][:, :], a[L1 + "ca_bv"])]
        m.ctx_wk = [(w[L0 + "w_kv"][:, :, 0:C], L0 + "w_kv"), (w[L1 + "ca_wk"][:, :, :], L1 + "ca_wk")]
        m.ctx_wv = [(w[L0 + "w_kv"][:, :, C:2 * C], L0 + "w_kv"), (w[L1 + "ca_wv"][:, :, :], L1 + "ca_wv")]
        m.ctx_k_bias = [col[L0 + "b_kv"], col[L1 + "ca_bk"]]
        m.ctx_v_row = [v_rows[1], v_rows[3]]

        def scale_shift(i):
            return lambda b: (m.mod[:, (3 * i + 1) * CK:(3 * i + 2) * CK, b], m.mod[:, 3 * i * CK:(3 * i + 1) * CK, b])

        def affine(g, b_):
            return lambda b: (col[g][:, :], col[b_][:, :])

        with ExitStack() as early:
            w_m1 = early.enter_context(nc.sbuf_tensor("w_m1", [P, CK, 2 * HID], F32))
            w_m2 = [early.enter_context(nc.sbuf_tensor(f"w_m2_{b}", [P, HID // P, C], F32)) for b in range(B)]
            m.weights = [(name, w[name][:, :, :]) for name, _ in order] + [(L0 + "w_m2", w_m2[1][:, :, :]), (L0 + "w_m1", w_m1[:, :, :])]
            m.w_in = {name: sem("in_" + name) for name in [n for n, _ in m.weights] + [L1 + "w1", L1 + "w2"]}
            m.gated = [(L0 + "w_so", w[L0 + "w_so"], (w_so2, w[L0 + "w_so"])), (L0 + "w_co", w[L0 + "w_co"], (w_co2, w[L0 + "w_co"])),
                       (L0 + "w_m2", w_m2[1], (w_m2[0], w_m2[1]))]
            modulation_stage(nc, m, a)
            context_stage(nc, m, a)

            qkv, bq = w[L0 + "w_qkv"], col[L0 + "b_qkv"]
            projection_stage(nc, m, "p1_", {
                "attended": False, "eps": 1e-6, "modulate": scale_shift(0), "w_name": L0 + "w_qkv", "w_more": (),
                "qk": [(qkv, h * P, bq[:, h:h + 1], SCALE, m.q_dram, h) for h in range(CK)]
                + [(qkv, C + h * P, bq[:, CK + h:CK + h + 1], 1.0, m.k_dram, h) for h in range(CK)],
                "v": (qkv, 2 * C), "v_row": v_rows[0][:, :]})
            short_attention_stage(nc, m, "a1_", "window")
            projection_stage(nc, m, "p2_", {
                "attended": True, "eps": 1e-6, "modulate": scale_shift(1), "w_name": L0 + "w_q", "w_more": (), "row": 0,
                "w_out": (w_so2, w[L0 + "w_so"]), "w_out_name": L0 + "w_so",
                "qk": [(w[L0 + "w_q"], h * P, col[L0 + "b_q"][:, h:h + 1], SCALE, m.q_dram, h) for h in range(CK)],
                "v": None})
            short_attention_stage(nc, m, "a2_", "topk")
            mlp_stage(nc, m, "p3_", {
                "attended": True, "eps": 1e-6, "modulate": scale_shift(2), "row": 1, "w_out": (w_co2, w[L0 + "w_co"]),
                "w_out_name": L0 + "w_co", "gated": True, "w_up": w_m1, "w_down": w_m2, "b_up": col[L0 + "b_m1"],
                "up_name": L0 + "w_m1", "down_name": L0 + "w_m2", "out": None})
        w1, w2 = sb("w1", [P, CK, HID]), sb("w2", [P, HID // P, C])
        with nc.Block() as block:

            @block.sync
            def _(sp):
                sp.dma_start(w1[:, :, :], a[L1 + "w1"].rearrange("(k p) n -> p k n", p=P)).then_inc(m.w_in[L1 + "w1"], 16)
                sp.dma_start(w2[:, :, :], a[L1 + "w2"].rearrange("(k p) n -> p k n", p=P)).then_inc(m.w_in[L1 + "w2"], 16)

        projection_stage(nc, m, "p4_", {
            "attended": False, "eps": 1e-5, "modulate": affine(L1 + "ln1_g", L1 + "ln1_b"), "w_name": L1 + "sa_wq",
            "w_more": (L1 + "sa_wk", L1 + "sa_wv"),
            "qk": [(w[L1 + "sa_wq"], h * P, col[L1 + "sa_bq"][:, h:h + 1], SCALE, m.q_dram, h) for h in range(CK)]
            + [(w[L1 + "sa_wk"], h * P, col[L1 + "sa_bk"][:, h:h + 1], 1.0, m.k_dram, h) for h in range(CK)],
            "v": (w[L1 + "sa_wv"], 0), "v_row": v_rows[2][:, :]})
        full_attention_stage(nc, m, "a3_")
        projection_stage(nc, m, "p5_", {
            "attended": True, "eps": 1e-5, "modulate": affine(L1 + "ln3_g", L1 + "ln3_b"), "w_name": L1 + "ca_wq", "w_more": (), "row": 3,
            "w_out": (w[L1 + "sa_wo"],) * B, "w_out_name": L1 + "sa_wo",
            "qk": [(w[L1 + "ca_wq"], h * P, col[L1 + "ca_bq"][:, h:h + 1], SCALE, m.q_dram, h) for h in range(CK)],
            "v": None})
        short_attention_stage(nc, m, "a4_", "masked")
        mlp_stage(nc, m, "p6_", {
            "attended": True, "eps": 1e-5, "modulate": affine(L1 + "ln2_g", L1 + "ln2_b"), "row": 4, "w_out": (w[L1 + "ca_wo"],) * B,
            "w_out_name": L1 + "ca_wo", "gated": False, "w_up": w1, "w_down": (w2, w2), "b_up": col[L1 + "b1"],
            "up_name": L1 + "w1", "down_name": L1 + "w2", "out": out})


def kernel(**inputs):
    import numpy as _np
    import concourse.bacc as _bacc
    from concourse import mybir as _mybir
    from concourse.bass_utils import run_bass_kernel_spmd as _run

    nc = _bacc.Bacc("TRN2", target_bir_lowering=False, num_devices=1)
    arrays, aps = {}, {}
    inputs = {name: _np.asarray(value) for name, value in inputs.items()}
    inputs["columns"] = _np.concatenate([inputs[name].reshape(n, P).T for name, n in COLUMNS], axis=1)
    inputs["cond_columns"] = inputs.pop("cond_1024").reshape(B, CK, P).transpose(2, 1, 0)
    inputs["mask_columns"] = inputs["mask_BxS2_ik0"].T
    for name, value in inputs.items():
        value = _np.ascontiguousarray(value)
        arrays["in_" + name] = value
        aps[name] = nc.dram_tensor("in_" + name, value.shape, _mybir.dt.from_np(value.dtype), kind="ExternalInput").ap()
    out = nc.dram_tensor("out_x", (B, L, C), F32, kind="ExternalOutput").ap()
    build(nc, aps, out)
    r = _run(nc, [arrays], core_ids=[0])
    return r.results[0]["out_x"]
```
